# Optimizing a Trainium2 kernel written in Bass

```python
import numpy as np
import jax
import jax.numpy as jnp

def _softmax(x, axis=-1):
    return jax.nn.softmax(x, axis=axis)

def _gelu(x):
    return jax.nn.gelu(x, approximate=True)

def _silu(x):
    return jax.nn.silu(x)

def _sigmoid(x):
    return jax.nn.sigmoid(x)

def _layernorm(x, axis=-1, eps=1e-05):
    m = jnp.mean(x, axis=axis, keepdims=True)
    v = jnp.var(x, axis=axis, keepdims=True)
    return (x - m) / jnp.sqrt(v + eps)

def _scatter_add(tgt, idx, src, axis=0):
    return tgt.at[idx].add(src)

def _segment_sum(src, seg, n):
    return jax.ops.segment_sum(src, seg, n)
kernel_name = 'mk_xattn_ffn_d1_seqx_r4_a4984a'

def setup_inputs(seed: int=0):
    np.random.seed(seed)
    _w = jnp.asarray

    def _rec_inputs():
        import jax
        import jax.numpy as jnp
        _rk = jax.random.key(seed)
        x = -0.0002928 + 1 * jax.random.normal(jax.random.fold_in(_rk, 1), (16, 128, 512), jnp.float32)
        _lenS = 128 - jax.random.randint(jax.random.fold_in(_rk, 7), (16,), 0, max(1, 128 // 4) + 1, jnp.int32)
        _lenS2 = 128 - jax.random.randint(jax.random.fold_in(_rk, 8), (16,), 0, max(1, 128 // 4) + 1, jnp.int32)
        _ctx_2048P = jax.random.normal(jax.random.fold_in(_rk, 11), (16, 16, 512), jnp.float32)
        _ctx_2048c = jax.random.dirichlet(jax.random.fold_in(_rk, 511), 0.3 * jnp.ones((16,), jnp.float32), (16, 128))
        _ctx_2048t = jnp.einsum('bsk,bkd->bsd', _ctx_2048c, _ctx_2048P)
        _ctx_2048t = _ctx_2048t * jax.lax.rsqrt(jnp.mean(jnp.square(_ctx_2048t)) + 1e-12) * 0.953939
        ctx_2048 = -1.39393e-06 + 0.999914 * (_ctx_2048t + 0.3 * jax.random.normal(jax.random.fold_in(_rk, 611), (16, 128, 512), jnp.float32))
        return (x, ctx_2048)
    x, ctx_2048 = _rec_inputs()

    def _L0_xattn_setup():
        import math
        import jax, jax.numpy as jnp
        import numpy as np
        N_HEADS = 8
        CHANNELS = 128
        K_CH = CHANNELS // N_HEADS
        THETA = 10000.0

        def _rope_freqs(length, dim):
            inv_freq = 1.0 / THETA ** (jnp.arange(0, dim, 2, dtype=jnp.float32) / dim)
            f = jnp.arange(length, dtype=jnp.float32)[:, None] * inv_freq[None, :]
            return jnp.concatenate([f, f], axis=-1)

        def _apply_rotary(pos, t):
            half = t.shape[-1] // 2
            rot = jnp.concatenate([-t[..., half:], t[..., :half]], axis=-1)
            return t * jnp.cos(pos) + rot * jnp.sin(pos)

        def _proj(inp, W, b):
            return jnp.einsum('oc,bct->bot', W, inp) + b[None, :, None]
        key = jax.random.key(seed)
        ks = jax.random.split(key, 10)
        B, C, T = (4, CHANNELS, 512)
        bound = math.sqrt(6.0 / (C + C))

        def w(k):
            return jax.random.uniform(k, (C, C), jnp.float32, -bound, bound)
        return {'x': jax.random.normal(ks[0], (B, C, T), jnp.float32), 'c': jax.random.normal(ks[1], (B, C, T), jnp.float32), 'Wq': w(ks[2]), 'bq': jnp.zeros((C,), jnp.float32), 'Wk': w(ks[3]), 'bk': jnp.zeros((C,), jnp.float32), 'Wv': w(ks[4]), 'bv': jnp.zeros((C,), jnp.float32), 'Wo': w(ks[5]), 'bo': jnp.zeros((C,), jnp.float32)}
    _L0_xattn_all = _L0_xattn_setup()
    _L0_xattn_in = {k: v for k, v in _L0_xattn_all.items() if k in ('Wq', 'bq', 'Wk', 'bk', 'Wv', 'bv', 'Wo', 'bo')}
    del _L0_xattn_all

    def _L0_ffn_setup():
        import jax, jax.numpy as jnp
        import numpy as np
        TOP_K = 8

        def _masked_routing(router_logits):
            T, E = router_logits.shape
            sel_w, sel_e = jax.lax.top_k(router_logits, TOP_K)
            sel_w = jax.nn.softmax(sel_w.astype(jnp.float32), axis=1)
            rows = jnp.arange(T)[:, None]
            masked = jnp.zeros((T, E), dtype=jnp.float32).at[rows, sel_e].set(sel_w)
            count = jnp.zeros((E,), dtype=jnp.int32).at[sel_e.reshape(-1)].add(1)
            return (masked, count)
        key = jax.random.key(seed)
        k1, k2, k3, k4, k5 = jax.random.split(key, 5)
        B, S, H, E, I = (1, 512, 512, 32, 192)
        return {'hidden_states': jax.random.normal(k1, (B, S, H), dtype=jnp.float32), 'gate_w': jax.random.normal(k2, (E, H), dtype=jnp.float32) * H ** (-0.5), 'w_gate_proj': jax.random.normal(k3, (E, I, H), dtype=jnp.float32) * H ** (-0.5), 'w_up_proj': jax.random.normal(k4, (E, I, H), dtype=jnp.float32) * H ** (-0.5), 'w_down_proj': jax.random.normal(k5, (E, H, I), dtype=jnp.float32) * I ** (-0.5)}
    _L0_ffn_all = _L0_ffn_setup()
    _L0_ffn_in = {k: v for k, v in _L0_ffn_all.items() if k in ('gate_w', 'w_gate_proj', 'w_up_proj', 'w_down_proj')}
    del _L0_ffn_all
    return {'x': x, 'ctx_2048': ctx_2048, 'L0_xattn_Wq': _L0_xattn_in['Wq'], 'L0_xattn_bq': _L0_xattn_in['bq'], 'L0_xattn_Wk': _L0_xattn_in['Wk'], 'L0_xattn_bk': _L0_xattn_in['bk'], 'L0_xattn_Wv': _L0_xattn_in['Wv'], 'L0_xattn_bv': _L0_xattn_in['bv'], 'L0_xattn_Wo': _L0_xattn_in['Wo'], 'L0_xattn_bo': _L0_xattn_in['bo'], 'L0_ffn_gate_w': _L0_ffn_in['gate_w'], 'L0_ffn_w_gate_proj': _L0_ffn_in['w_gate_proj'], 'L0_ffn_w_up_proj': _L0_ffn_in['w_up_proj'], 'L0_ffn_w_down_proj': _L0_ffn_in['w_down_proj']}

def reference(x, ctx_2048, L0_xattn_Wq, L0_xattn_bq, L0_xattn_Wk, L0_xattn_bk, L0_xattn_Wv, L0_xattn_bv, L0_xattn_Wo, L0_xattn_bo, L0_ffn_gate_w, L0_ffn_w_gate_proj, L0_ffn_w_up_proj, L0_ffn_w_down_proj):
    import jax
    import jax.numpy as jnp

    def _L0_xattn_ref(x, c, Wq, bq, Wk, bk, Wv, bv, Wo, bo):
        import math
        import jax, jax.numpy as jnp
        import numpy as np
        N_HEADS = 8
        CHANNELS = 128
        K_CH = CHANNELS // N_HEADS
        THETA = 10000.0

        def _rope_freqs(length, dim):
            inv_freq = 1.0 / THETA ** (jnp.arange(0, dim, 2, dtype=jnp.float32) / dim)
            f = jnp.arange(length, dtype=jnp.float32)[:, None] * inv_freq[None, :]
            return jnp.concatenate([f, f], axis=-1)

        def _apply_rotary(pos, t):
            half = t.shape[-1] // 2
            rot = jnp.concatenate([-t[..., half:], t[..., :half]], axis=-1)
            return t * jnp.cos(pos) + rot * jnp.sin(pos)

        def _proj(inp, W, b):
            return jnp.einsum('oc,bct->bot', W, inp) + b[None, :, None]
        b, _, t_t = x.shape
        t_s = c.shape[2]
        q_emb = _rope_freqs(t_t, K_CH)
        k_emb = _rope_freqs(t_s, K_CH)

        def split_heads(t):
            return t.reshape(b, N_HEADS, K_CH, t.shape[2]).transpose(0, 1, 3, 2)
        q = split_heads(_proj(x, Wq, bq))
        k = split_heads(_proj(c, Wk, bk))
        v = split_heads(_proj(c, Wv, bv))
        q = _apply_rotary(q_emb, q)
        k = _apply_rotary(k_emb, k)
        scores = jnp.einsum('bhtc,bhsc->bhts', q, k) / math.sqrt(K_CH)
        p_attn = jax.nn.softmax(scores, axis=-1)
        out = jnp.einsum('bhts,bhsc->bhtc', p_attn, v)
        out = out.transpose(0, 1, 3, 2).reshape(b, N_HEADS * K_CH, t_t)
        return _proj(out, Wo, bo)

    def _L0_ffn_ref(hidden_states, gate_w, w_gate_proj, w_up_proj, w_down_proj):
        import jax, jax.numpy as jnp
        import numpy as np
        TOP_K = 8

        def _masked_routing(router_logits):
            T, E = router_logits.shape
            sel_w, sel_e = jax.lax.top_k(router_logits, TOP_K)
            sel_w = jax.nn.softmax(sel_w.astype(jnp.float32), axis=1)
            rows = jnp.arange(T)[:, None]
            masked = jnp.zeros((T, E), dtype=jnp.float32).at[rows, sel_e].set(sel_w)
            count = jnp.zeros((E,), dtype=jnp.int32).at[sel_e.reshape(-1)].add(1)
            return (masked, count)
        B, S, H = hidden_states.shape
        x = hidden_states.reshape(-1, H)
        router_logits = x @ gate_w.T
        masked_w, _count = _masked_routing(router_logits)
        g = jnp.einsum('th,eih->tei', x, w_gate_proj)
        u = jnp.einsum('th,eih->tei', x, w_up_proj)
        h = jax.nn.silu(g) * u
        h = h * masked_w[:, :, None]
        out = jnp.einsum('tei,ehi->th', h, w_down_proj)
        return out.reshape(B, S, H)
    x = x + _L0_xattn_ref(_layernorm(x, axis=-1), ctx_2048, L0_xattn_Wq, L0_xattn_bq, L0_xattn_Wk, L0_xattn_bk, L0_xattn_Wv, L0_xattn_bv, L0_xattn_Wo, L0_xattn_bo)
    x = x + _L0_ffn_ref(_layernorm(x, axis=-1), L0_ffn_gate_w, L0_ffn_w_gate_proj, L0_ffn_w_up_proj, L0_ffn_w_down_proj)
    return x

_drawn_inputs = setup_inputs


def setup_inputs(seed=0):
    import zlib

    import numpy as np

    out = dict(_drawn_inputs(seed))
    spreads = {'L0_xattn_bq': (0.0, 0.282),
     'L0_xattn_bk': (0.0, 0.456),
     'L0_xattn_bv': (0.0, 0.1),
     'L0_xattn_bo': (0.0, 0.1)}
    factors = {}
    for name, (base, spread) in spreads.items():
        noise = np.random.default_rng([zlib.crc32(name.encode()), seed]).standard_normal(out[name].shape)
        drawn = base * np.exp(spread * noise) if base else spread * noise
        out[name] = jnp.asarray(drawn.astype(out[name].dtype))
    for name, factor in factors.items():
        out[name] = (out[name] * factor).astype(out[name].dtype)
    return out
```

```python
import concourse.bass as bass
from concourse import mybir
from contextlib import ExitStack
import numpy as np

F32, F16, U32, I32 = mybir.dt.float32, mybir.dt.float16, mybir.dt.uint32, mybir.dt.int32
ALU = mybir.AluOpType
ACT = mybir.ActivationFunctionType
AXX = mybir.AxisListType.X

P = 128
T = 512
HEADS, DH = 8, 16
E, INTER, TOPK = 32, 192, 8
KT = T // P
NSC = T // P
WCOLS = KT * 2 * INTER + 2 * T
DOWN = KT * 2 * INTER
WSCALE = 64.0
PSCALE = 8.0
MSCALE = 32.0
EPS = 1e-5
SLOTS = 4
STEP_FIELDS = 8
SHARE = 2 * DH + DH
HI, LO = 0, 1
COS, SIN, EXPERT, EXPERT_ROW, STEP_NO, TOKEN, HALF, NCONST = 0, T, 2 * T, 2 * T + E, 2 * T + 2 * E, 2 * T + 2 * E + 2, 2 * T + 2 * E + 3, 2 * T + 2 * E + 4


class Turn:

    def __init__(self, k, off, group, limit):
        self.k, self.off, self.group, self.limit = k, off, group, limit

    def __add__(self, d):
        return Turn(self.k, self.off + d, self.group, self.limit)

    def slot(self, n):
        return self.off % n

    def live(self):
        return not isinstance(self.k, int) or 0 <= self.group * self.k + self.off < self.limit

    def count(self, a, c=0):
        return self.k * (a * self.group) + (a * self.off + c)

    def rounds(self, a, c=0):
        return self.k * a + (a * (self.off // self.group) + c)


def need(eng, sem, value):
    if isinstance(value, int) and value <= 0:
        return
    eng.wait_ge(sem, value)


def of(ap, b):
    n = b.count(1)
    return ap[n] if isinstance(n, int) else ap[bass.ds(n, 1)].squeeze(0)


def xattn_moe(nc, x, ctx, proj_w, proj_b, value_b, out_w, gate_w, expert_w, const_f, const_h, out):
    NB = x.shape[0]
    TOKENS = NB * P
    STEPS = TOKENS * TOPK // P + E
    EROWS = TOKENS
    TABLE_ROWS = -(-(E * EROWS + (STEPS + 4) * P) // P) * P
    assert STEPS % 4 == 0 and NB % 2 == 0

    q_stack_d = nc.dram_tensor("qk_parts", (NB, 4, P, T), F16).ap()
    den_d = nc.dram_tensor("denominators", (NB, 2, 4, T), F32).ap()
    rcp_d = nc.dram_tensor("reciprocals", (NB, 2, 4, T), F32).ap()
    tok_d = nc.dram_tensor("normalised_tokens", (TOKENS, 2 * T), F16).ap()
    rows_d = nc.dram_tensor("expert_rows", (TABLE_ROWS, 4), U32).ap()
    steps_d = nc.dram_tensor("step_table", (2 * P, STEP_FIELDS), I32).ap()
    started_d = nc.dram_tensor("started_out", (4, 4), F32).ap()
    out_rows = out.rearrange("b c t -> (b c) t")

    ctxs = ExitStack()
    with ctxs:
        def sb(name, shape, dt):
            return ctxs.enter_context(nc.sbuf_tensor(name, shape, dt))

        def sem(name):
            return ctxs.enter_context(nc.semaphore(name))

        cf = sb("cf", [P, NCONST], F32)
        ch = sb("ch", [P, 3, P], F16)
        ident, before, ones = ch[:, 0, :], ch[:, 1, :], ch[:, 2, :]
        pw = sb("pw", [P, 5, P], F32)
        pws = sb("pws", [P, 2, 5, P], F16)
        pb = sb("pb", [P, 4], F32)
        vb = sb("vb", [P, P], F32)
        ow = sb("ow", [P, 2, P], F32)
        ows = sb("ows", [P, 2, 2, P], F16)
        gw = sb("gw", [P, KT, E], F32)
        gws = sb("gws", [P, 2, KT, E], F16)
        w_lo = sb("w_lo", [P, SLOTS * WCOLS], F16)
        places_of_inputs = w_lo[:, :].rearrange("p (n t) -> p n t", n=5)
        x_in, c_in, x_res = (places_of_inputs[:, n, :].bitcast(F32).rearrange("p (s t) -> p s t", s=2) for n in range(3))
        xs, cs = (places_of_inputs[:, n, :].rearrange("p (s a t) -> p s a t", s=2, a=2) for n in (3, 4))
        xn = sb("xn", [P, T], F32)
        stat = sb("stat", [P, 2, 8], F32)
        mv = sb("mv", [P, 2, 2], F32)
        vare = sb("vare", [P, 2], F32)
        rstd = sb("rstd", [P, 2], F32)
        rope_a = sb("rope_a", [P, 2, T], F32)
        rope_b = sb("rope_b", [P, 2, T], F32)
        rope_s = sb("rope_s", [P, 2, T], F32)
        qk = sb("qk", [P, 4, T], F16)
        q_st = sb("q_st", [64, 2, HEADS, T], F16)
        k_st = sb("k_st", [64, 2, HEADS, T], F16)
        mx = sb("mx", [P, 2, HEADS, NSC], F32)
        mneg = sb("mneg", [P, 2, HEADS * NSC], F16)
        mrow = sb("mrow", [16, 2, P], F16)
        v1 = sb("v1", [P, 2, NSC, HEADS, 2 * DH], F32)
        pr = sb("pr", [P, 8, T], F32)
        o_raw = sb("o_raw", [P, 2, T], F32)
        den = sb("den", [P, 2, 16], F32)
        rcp = sb("rcp", [P, 2, 16], F32)
        rcb = sb("rcb", [P, 2, T], F32)
        o_n = sb("o_n", [P, 2, T], F32)
        o_s = sb("o_s", [P, 2, 2, T], F16)
        x2 = sb("x2", [P, 2, T], F32)
        xn2 = sb("xn2", [P, T], F32)
        x2s = sb("x2s", [P, 2, 2, T], F16)
        x2t = sb("x2t", [P, 8, P], F16)
        lg = sb("lg", [P, E], F32)
        top = sb("top", [P, 8], F32)
        topi = sb("topi", [P, 8], U32)
        topf = sb("topf", [P, 8], F32)
        ntop = sb("ntop", [P, 1], F32)
        ex = sb("ex", [P, 8], F32)
        exs = sb("exs", [P, 1], F32)
        exr = sb("exr", [P, 1], F32)
        chosen = sb("chosen", [P, TOPK, E], F32)
        placed = sb("placed", [P, TOPK, E], F32)
        mask = sb("mask", [P, E], F16)
        place = sb("place", [P, E], F32)
        running = sb("running", [P, E], F32)
        rowi = sb("rowi", [P, 2, TOPK], U32)
        rows = sb("rows", [P, 2, TOPK, 4], U32)
        started = sb("started", [1, 4], F32)
        tokf = sb("tokf", [P, 1], F32)
        zero = sb("zero", [P, 2 * TOPK], F32)
        plan = sb("plan", [P, 12, E], F32)
        plani = sb("plani", [P, E], I32)
        col = sb("col", [P, 2, 16], F32)
        coli = sb("coli", [P, 2, 4], I32)
        stepi = sb("stepi", [P, 2, STEP_FIELDS], I32)
        tab = sb("tab", [1, 2 * P * STEP_FIELDS], I32)
        stage = sb("stage", [P, 2 * WCOLS], F32)
        w_hi = sb("w_hi", [P, SLOTS * WCOLS], F16)

        pad_rows = w_hi[:, :].bitcast(U32)
        g_idx = sb("g_idx", [P, 4, 4], U32)
        s_idx = sb("s_idx", [P, 4, 4], U32)
        xg = pr[:, 0:4, :].bitcast(F16)
        xt = pr[:, 4:6, :].bitcast(F16)
        y_sb = v1[:, :, :, :, :].rearrange("p a b c d -> p (a b c d)").rearrange("p (r t) -> p r t", r=4)
        sil = rope_a[:, :, 0:INTER]
        hf = rope_b[:, :, 0:INTER]
        hs = rope_s[:, :, :].bitcast(F16)[:, :, 0:2 * INTER]
        ht = x2[:, :, :].bitcast(F16)[:, :, 0:3 * P].rearrange("p r (b t) -> p r b t", b=3)

        ps = ctxs.enter_context(nc.psum_tensor("ps", [P, 8, T], F32))
        ps_m = [ps[:, 0:2, :], ps[:, 2:4, :]]
        ps_s = [ps[:, 4, :], ps[:, 5, :]]
        ps_o = ps[:, 6, :]
        ps_x = ps[:, 7, :]
        ps_xh = ps_x.bitcast(F16)

        consts_in = sem("consts_in")
        x_loaded = [sem(f"x_loaded{i}") for i in range(2)]
        c_loaded = [sem(f"c_loaded{i}") for i in range(2)]
        res_loaded = [sem(f"res_loaded{i}") for i in range(2)]
        pads_stored = sem("pads_stored")
        setup = sem("setup")
        pads_set = sem("pads_set")
        w_split = sem("w_split")
        mx_done, mneg_done = sem("mx_done"), sem("mneg_done")
        rope_done, v_done, x2_done = sem("rope_done"), sem("v_done"), sem("x2_done")
        stat1, stat2 = sem("stat1"), sem("stat2")
        xn_done, xn2_done = sem("xn_done"), sem("xn2_done")
        rcp_done, on_done = sem("rcp_done"), sem("on_done")
        lg_done, rt, mask_done, cnt_done, rows_done = sem("lg_done"), sem("rt"), sem("mask_done"), sem("cnt_done"), sem("rows_done")
        ntop_done = sem("ntop_done")
        exp_done, o_read = sem("exp_done"), sem("o_read")
        mrow_done = sem("mrow_done")
        qk_hi, xc_hi, on_hi, x2_hi, xt_read, ex_done = sem("qk_hi"), sem("xc_hi"), sem("on_hi"), sem("x2_hi"), sem("xt_read"), sem("ex_done")
        rstd1, rstd2 = sem("rstd1"), sem("rstd2")
        rope_sum, qk_lo, xc_lo, on_lo, x2_lo = sem("rope_sum"), sem("qk_lo"), sem("xc_lo"), sem("on_lo"), sem("x2_lo")
        rows_stored = [sem(f"rows_stored{i}") for i in range(2)]
        proj_mm, v_mm, y_mm, xt_mm, lg_mm, cnt_mm, mt_mm = (sem(n) for n in ("proj_mm", "v_mm", "y_mm", "xt_mm", "lg_mm", "cnt_mm", "mt_mm"))
        s1_mm, s2_mm, pv_mm = sem("s1_mm"), sem("s2_mm"), sem("pv_mm")
        qk_stored = sem("qk_stored")
        stack_in = [[sem(f"stack_in{p}{h}") for h in range(2)] for p in range(2)]
        mrow_in = [[sem(f"mrow_in{p}{h}") for h in range(2)] for p in range(2)]
        den_out, den_in, rcp_out, rcb_in = sem("den_out"), sem("den_in"), sem("rcp_out"), [sem(f"rcb_in{g}") for g in range(2)]
        x2_stored = [sem(f"x2_stored{i}") for i in range(2)]
        tok_stored = [sem(f"tok_stored{i}") for i in range(2)]

        def apart(eng):
            eng.sem_inc(passed, 1)

        def batch_turns(eng, body):
            first = 3
            pairs = max(0, (NB - 4 - first) // 2)
            for n in range(-4, first):
                body(Turn(n // 2, n % 2, 2, NB))
            if pairs > 0:
                with eng.Fori(first // 2, first // 2 + pairs, 1) as k:
                    for u in range(2):
                        body(Turn(k, first % 2 + u, 2, NB))
            for n in range(first + 2 * pairs, NB + 4):
                body(Turn(n // 2, n % 2, 2, NB))

        def tenants(it):
            return [("q", it + 2, rope_done, (it + 2).count(4, 1)),
                    ("mt1", it, mrow_done, it.count(2, 2)),
                    ("qr", it + 2, rope_done, (it + 2).count(4, 2)),
                    ("k", it + 2, rope_done, (it + 2).count(4, 3)),
                    ("kr", it + 2, rope_done, (it + 2).count(4, 4)),
                    ("xt", it + -2, xt_read, (it + -2).count(1, 1)),
                    ("mt0", it + 1, mrow_done, (it + 1).count(2, 1)),
                    ("v", it + 1, v_done, (it + 1).count(1, 1)),
                    ("lg", it + -2, lg_done, (it + -2).count(1, 1)),
                    ("cnt", it + -2, cnt_done, (it + -2).count(2, 2)),
                    ("y", it + -1, x2_done, (it + -1).count(1, 1))]

        def bank_is_free(eng, it, name):
            order = tenants(it + -1) + tenants(it)
            at = len(order) // 2 + [n for n, *_ in tenants(it)].index(name)
            for _, batch, reader, value in reversed(order[:at]):
                if batch.live():
                    need(eng, reader, value)
                    return

        idx_in = [sem(f"idx_in{i}") for i in range(4)]
        sidx_in = [sem(f"sidx_in{i}") for i in range(4)]
        gathered = [sem(f"gathered{i}") for i in range(4)]
        added = [sem(f"added{i}") for i in range(4)]
        w_in = sem("w_in")
        gu_mm, ht_mm, d_mm, xgt_mm = sem("gu_mm"), sem("ht_mm"), sem("d_mm"), sem("xgt_mm")
        xt_out, h_done, hlo_done = sem("xt_out"), sem("h_done"), sem("hlo_done")
        sil_done, hhi_done, ht_out, y_out = sem("sil_done"), sem("hhi_done"), sem("ht_out"), sem("y_out")
        plan_sem, tab_out, tab_in, attn_end = sem("plan_sem"), sem("tab_out"), sem("tab_in"), sem("attn_end")
        gp_init = sem("gp_init")
        passed = sem("passed")

        block = ctxs.enter_context(nc.Block())

        def step_loop(eng, body):
            for u in range(4):
                body(Turn(0, 1 + u, 4, STEPS + 8))
            with eng.Fori(1, STEPS // 4, 1) as i:
                for u in range(4):
                    body(Turn(i, 1 + u, 4, STEPS + 8))

        def field(eng, s, f, lo, hi):
            at = s.count(STEP_FIELDS, f)
            view = tab[0:1, at:at + 1] if isinstance(at, int) else tab[0:1, bass.ds(at, 1)]
            return eng.value_load(view, min_val=lo, max_val=hi)

        PLAN_STEPS = 37

        @block.sync
        def _(sp):
            for dst, src in ((cf[:, :], const_f), (ch[:, :, :], const_h), (pw[:, :, :], proj_w), (pb[:, :], proj_b),
                             (vb[:, :], value_b), (ow[:, :, :], out_w), (gw[:, :, :], gate_w)):
                sp.dma_start(dst, src).then_inc(consts_in, 16)

            def turn(it):
                bi, bp, b1, b2, bo, br = it + 4, it + 2, it + 1, it, it + -1, it + -2
                if bi.live():
                    need(sp, xn_done, bi.count(1, -1))
                    need(sp, xc_lo, bi.count(1, -1))
                    sp.dma_start(x_in[:, bi.slot(2), :], of(x, bi)).then_inc(x_loaded[bi.slot(2)], 16)
                    sp.dma_start(c_in[:, bi.slot(2), :], of(ctx, bi)).then_inc(c_loaded[bi.slot(2)], 16)
                if b2.live():
                    need(sp, x2_done, b2.count(1, -1))
                    sp.dma_start(x_res[:, b2.slot(2), :], of(x, b2)).then_inc(res_loaded[b2.slot(2)], 16)
                if b1.live():
                    load_stack(b1, 1)
                if b2.live():
                    store_mrow(b2, 1)
                if bo.live():
                    den_round(bo, 1)
                if br.live():
                    sp.wait_ge(x2_lo, br.count(1, 1))
                    sp.dma_start(of(out, br), x2[:, br.slot(2), :]).then_inc(x2_stored[br.slot(2)], 16)
                    sp.dma_start(tok_rows(br), x2s[:, br.slot(2), :, :].rearrange("p a t -> p (a t)")).then_inc(tok_stored[br.slot(2)], 16)
                if bo.live():
                    rcp_round(bo, 1)
                if b1.live():
                    store_mrow(b1, 0)
                if bp.live():
                    sp.wait_ge(qk_lo, bp.count(2, 2))
                    sp.dma_start(of(q_stack_d, bp).rearrange("a p t -> p a t"), qk[:, :, :]).then_inc(qk_stored, 16)
                if b2.live():
                    den_round(b2, 0)
                if bp.live():
                    sp.wait_ge(qk_stored, bp.count(16, 16))
                    load_stack(bp, 0)
                if b2.live():
                    rcp_round(b2, 0)

            def tok_rows(b):
                at = b.count(P)
                return tok_d[at:at + P, :] if isinstance(at, int) else tok_d[bass.ds(at, P), :]

            def load_stack(b, half):
                need(sp, s2_mm, b.count(32, -64 + 16 * (half + 1)))
                heads = slice(4 * half, 4 * half + 4)
                for st, parts in ((q_st, (0, 0, 1)), (k_st, (2, 3, 2))):
                    for r, part in enumerate(parts):
                        src = of(q_stack_d, b)[part].rearrange("(h c) t -> c h t", c=DH)[:, heads, :]
                        sp.dma_start(st[DH * r:DH * (r + 1), b.slot(2), heads, :], src).then_inc(stack_in[b.slot(2)][half], 16)

            def store_mrow(b, half):
                sp.wait_ge(mrow_done, b.count(2, half + 1))
                sp.dma_start(q_st[SHARE:SHARE + 1, b.slot(2), 4 * half:4 * half + 4, :].rearrange("p h (j t) -> p (h j) t", j=NSC),
                             mrow[:, half, :]).then_inc(mrow_in[b.slot(2)][half], 16)

            def den_round(b, g):
                sp.wait_ge(o_read, b.count(2, g + 1))
                sp.dma_start(of(den_d, b)[g], o_raw[DH:P:2 * DH, g, :]).then_inc(den_out, 16)
                sp.wait_ge(den_out, b.count(32, 16 * g + 16))
                sp.dma_start(den[:, g, :], of(den_d, b)[g].rearrange("j (a t) -> (j a) t", t=16)).then_inc(den_in, 16)

            def rcp_round(b, g):
                sp.wait_ge(rcp_done, b.count(2, g + 1))
                sp.dma_start(of(rcp_d, b)[g].rearrange("j (a t) -> (j a) t", t=16), rcp[:, g, :]).then_inc(rcp_out, 16)
                sp.wait_ge(rcp_out, b.count(32, 16 * g + 16))
                apart(sp)
                need(sp, on_done, b.count(2, g - 1))
                apart(sp)
                for j in range(4):
                    row = of(rcp_d, b)[g, j:j + 1, :]
                    sp.dma_start(rcb[2 * DH * j:2 * DH * (j + 1), g, :], row.to_broadcast([2 * DH, T])).then_inc(rcb_in[g], 16)

            batch_turns(sp, turn)
            for n in range(2):
                sp.wait_ge(w_in, 16 * n) if n else None
                sp.dma_start(stage[:, n * WCOLS:(n + 1) * WCOLS], expert_w[n]).then_inc(w_in, 16)
            for p in range(2):
                sp.wait_ge(x2_stored[p], 16 * (NB // 2))
                sp.wait_ge(tok_stored[p], 16 * (NB // 2))
            sp.wait_ge(plan_sem, PLAN_STEPS)
            sp.dma_start(steps_d.rearrange("(q p) f -> p q f", p=P), stepi[:, :, :]).then_inc(tab_out, 16)
            sp.wait_ge(tab_out, 16)
            sp.dma_start(tab[:, :], steps_d.rearrange("(o s) f -> o (s f)", o=1)).then_inc(tab_in, 16)
            sp.wait_ge(tab_in, 16)
            for p in range(2):
                sp.wait_ge(rows_stored[p], 16 * TOPK * (NB // 2))

            def load_rows(s, ring, sems, d):
                row = field(sp, s + d, 0, 0, TABLE_ROWS - P)
                r = (s + d).slot(4)
                sp.dma_start(ring[:, r, :], rows_d[bass.ds(row, P), :]).then_inc(sems[r], 16)

            s0 = Turn(0, 0, 4, STEPS + 8)
            for d in range(4):
                load_rows(s0, g_idx, idx_in, d)
            for d in range(3):
                load_rows(s0, s_idx, sidx_in, d)
            sp.wait_ge(w_split, 2)
            sp.dma_start(stage[:, 0:WCOLS], expert_w[2]).then_inc(w_in, 16)

            def next_weights(s):
                first = field(sp, s + 1, 3, 0, 1)
                e1 = field(sp, s + 1, 2, 1, E)
                with sp.If(first > 0):
                    sp.wait_ge(w_split, e1 * 2)
                    sp.wait_ge(w_in, e1 * 16 + 16)
                    apart(sp)
                    at = field(sp, s + 1, 6, 0, WCOLS)
                    we = field(sp, s + 1, 7, 0, E - 1)
                    sp.dma_start(stage[:, bass.ds(at, WCOLS)],
                                 expert_w[bass.ds(we, 1), :, :].rearrange("e p c -> p (e c)")).then_inc(w_in, 16)
                with sp.Else():
                    sp.nop()
                sp.nop()

            next_weights(s0)

            def step(s):
                sp.wait_ge(gathered[s.slot(4)], s.rounds(16, 16))
                apart(sp)
                load_rows(s, g_idx, idx_in, 4)
                sp.wait_ge(added[(s + -1).slot(4)], (s + -1).rounds(16, 32))
                apart(sp)
                load_rows(s, s_idx, sidx_in, 3)
                next_weights(s)

            sp.wait_ge(gathered[0], 16)
            load_rows(s0, g_idx, idx_in, 4)
            load_rows(s0, s_idx, sidx_in, 3)
            step_loop(sp, step)
            for r in range(4):
                sp.wait_ge(added[r], 16 + 16 * (STEPS // 4))
                sp.wait_ge(idx_in[r], 16 * len(range(r, STEPS + 5, 4)))
                sp.wait_ge(sidx_in[r], 16 * len(range(r, STEPS + 4, 4)))
                sp.wait_ge(gathered[r], 16 * len(range(r, STEPS + 4, 4)))
            sp.wait_ge(w_in, 16 * (E + 2))

        @block.gpsimd
        def _(gp):
            sub = lambda o, a, b: nc.gpsimd.tensor_tensor(o, a, b, ALU.subtract)
            gp.wait_ge(pads_set, 2)
            gp.dma_start(rows_d.rearrange("(p r) f -> p (r f)", p=P), pad_rows[:, 0:TABLE_ROWS // P * 4]).then_inc(pads_stored, 16)
            gp.wait_ge(consts_in, 16 * 7)

            def scatter_rows(b, ks):
                if not b.live():
                    return
                if ks[0] == 0:
                    gp.wait_ge(pads_stored, 16)
                    gp.wait_ge(rows_done, b.count(3, 3))
                    apart(gp)
                for k in ks:
                    nc.gpsimd.indirect_dma_start(rows_d, bass.IndirectOffsetOnAxis(rowi[:, b.slot(2), k:k + 1], 0),
                                                 rows[:, b.slot(2), k, :], None).then_inc(rows_stored[b.slot(2)], 16)

            def turn(it):
                bl, bp, b2, bo, br, bs = it + 3, it + 2, it, it + -1, it + -2, it + -3
                scatter_rows(bs, (0, 1))
                if br.live():
                    gp.wait_ge(stat2, br.count(3, 3))
                    nc.gpsimd.tensor_tensor(rstd[:, 1:2], vare[:, 1:2], cf[:, HALF:HALF + 1], ALU.pow).then_inc(rstd2, 1)
                if bp.live():
                    rope_add(bp, 0)
                if bo.live():
                    low_of_o(bo, 0)
                if bp.live():
                    low_of_qk(bp, 0)
                if br.live():
                    gp.wait_ge(x2_hi, br.count(1, 1))
                    need(gp, tok_stored[br.slot(2)], br.rounds(16, 0))
                    sub(x2s[:, br.slot(2), LO, :], xn2[:, :], x2s[:, br.slot(2), HI, :]).then_inc(x2_lo, 1)
                scatter_rows(bs, (2, 3))
                if bl.live():
                    gp.wait_ge(stat1, bl.count(3, 3))
                    nc.gpsimd.tensor_tensor(rstd[:, 0:1], vare[:, 0:1], cf[:, HALF:HALF + 1], ALU.pow).then_inc(rstd1, 1)
                if bp.live():
                    rope_add(bp, 1)
                    low_of_qk(bp, 1)
                if bl.live():
                    gp.wait_ge(xc_hi, bl.count(2, 2))
                    need(gp, v_mm, bl.count(1, -1))
                    need(gp, proj_mm, bl.count(4, -4))
                    sub(xs[:, bl.slot(2), LO, :], xn[:, :], xs[:, bl.slot(2), HI, :])
                    sub(cs[:, bl.slot(2), LO, :], c_in[:, bl.slot(2), :], cs[:, bl.slot(2), HI, :]).then_inc(xc_lo, 1)
                scatter_rows(bs, (4, 5, 6, 7))
                if bo.live():
                    low_of_o(bo, 1)

            def rope_add(b, w):
                gp.wait_ge(rope_done, b.count(4, 2 * w + 2))
                need(gp, qk_lo, b.count(2, w - 1))
                nc.gpsimd.tensor_tensor(rope_s[:, w, :], rope_a[:, w, :], rope_b[:, w, :], ALU.add).then_inc(rope_sum, 1)

            def low_of_qk(b, w):
                gp.wait_ge(qk_hi, b.count(2, w + 1))
                need(gp, qk_stored, b.count(16, 0))
                sub(qk[:, 2 * w + LO, :], rope_s[:, w, :], qk[:, 2 * w + HI, :]).then_inc(qk_lo, 1)

            def low_of_o(b, g):
                gp.wait_ge(on_hi, b.count(2, g + 1))
                need(gp, y_mm, b.count(1))
                sub(o_s[:, g, LO, :], o_n[:, g, :], o_s[:, g, HI, :]).then_inc(on_lo, 1)

            batch_turns(gp, turn)

            gp.wait_ge(tab_in, 16)
            nc.gpsimd.memset(started[:, :], 0.0).then_inc(gp_init, 1)
            gp.wait_ge(gp_init, 1)
            for r in range(4):
                gp.dma_start(started_d[r:r + 1, :], started[:, :]).then_inc(added[r], 16)
            for p in range(2):
                gp.wait_ge(rows_stored[p], 16 * TOPK * (NB // 2))
                gp.wait_ge(tok_stored[p], 16 * (NB // 2))
                gp.wait_ge(x2_stored[p], 16 * (NB // 2))
            gp.wait_ge(xt_read, NB)
            gp.wait_ge(pv_mm, 8 * NB)

            def gather(s):
                r = s.slot(4)
                gp.wait_ge(idx_in[r], s.rounds(16, 16))
                need(gp, xgt_mm, s.count(1, -3))
                apart(gp)
                nc.gpsimd.indirect_dma_start(xg[:, r, :], None, tok_d, bass.IndirectOffsetOnAxis(g_idx[:, r, 0:1], 0)).then_inc(gathered[r], 16)

            s0 = Turn(0, 0, 4, STEPS + 8)
            for d in range(4):
                gather(s0 + d)

            def step(s):
                gather(s + 3)
                t = s + -1
                r = t.slot(4)
                gp.wait_ge(sidx_in[r], t.rounds(16, 16))
                gp.wait_ge(y_out, t.count(1, 1))
                base = field(gp, t, 4, 0, STEPS)
                for q in range(4):
                    gp.wait_ge(added[q], added_before(base, q))
                apart(gp)
                nc.gpsimd.indirect_dma_start(out_rows, bass.IndirectOffsetOnAxis(s_idx[:, r, 1:2], 0), y_sb[:, r, :], None,
                                             bounds_check=TOKENS - 1, oob_is_err=False, compute_op=ALU.add).then_inc(added[r], 16)

            def added_before(base, q):
                return ((base + (3 - q)) // 4) * 16 + 16

            step_loop(gp, step)

        @block.scalar
        def _(act):
            copy = lambda o, i, s=1.0: nc.scalar.activation(o, i, ACT.Copy, scale=s)
            act.wait_ge(consts_in, 16 * 7)

            def exps(b2, k):
                if not b2.live():
                    return
                for i in range(4):
                    n = 4 * k + i
                    act.wait_ge(s2_mm, b2.count(32, n + 1))
                    need(act, pv_mm, b2.count(8, n // 4 - 1))
                    nc.scalar.activation(pr[:, n % 8, :], ps_s[i % 2], ACT.Exp, scale=DH ** -0.5).then_inc(exp_done, 1)

            def read_o(b, g):
                act.wait_ge(pv_mm, b.count(8, 4 * g + 4))
                need(act, on_done, b.count(2, g - 1))
                need(act, den_out, b.count(32, 16 * g - 16))
                copy(o_raw[:, g, :], ps_o).then_inc(o_read, 1)

            def max_row(b, half):
                act.wait_ge(mt_mm, b.count(2, half + 1))
                need(act, mrow_in[(b + -1).slot(2)][half], (b + -1).rounds(16, 16))
                copy(mrow[:, half, :], ps_xh[0:16, 0:P]).then_inc(mrow_done, 1)

            def high_of_qk(b, w):
                act.wait_ge(rope_sum, b.count(2, w + 1))
                need(act, qk_stored, b.count(16, 0))
                copy(qk[:, 2 * w + HI, :], rope_s[:, w, :]).then_inc(qk_hi, 1)

            def high_of_o(b, g):
                act.wait_ge(on_done, b.count(2, g + 1))
                need(act, y_mm, b.count(1))
                copy(o_s[:, g, HI, :], o_n[:, g, :]).then_inc(on_hi, 1)

            def turn(it):
                bl, bp, b1, b2, bo, br = it + 3, it + 2, it + 1, it, it + -1, it + -2
                exps(b2, 0)
                if bo.live():
                    read_o(bo, 1)
                if b2.live():
                    max_row(b2, 1)
                exps(b2, 1)
                if bo.live():
                    high_of_o(bo, 0)
                if bp.live():
                    high_of_qk(bp, 0)
                exps(b2, 2)
                if br.live():
                    act.wait_ge(xn2_done, br.count(1, 1))
                    need(act, tok_stored[br.slot(2)], br.rounds(16, 0))
                    need(act, xt_mm, br.count(1, -1))
                    copy(x2s[:, br.slot(2), HI, :], xn2[:, :]).then_inc(x2_hi, 1)
                exps(b2, 3)
                if bp.live():
                    high_of_qk(bp, 1)
                exps(b2, 4)
                if b2.live():
                    read_o(b2, 0)
                if br.live():
                    act.wait_ge(xt_mm, br.count(1, 1))
                    need(act, lg_mm, br.count(1))
                    copy(x2t[:, :, :], ps_xh.rearrange("p (b t) -> p b t", b=8)).then_inc(xt_read, 1)
                if b1.live():
                    max_row(b1, 0)
                exps(b2, 5)
                if bl.live():
                    act.wait_ge(xn_done, bl.count(1, 1))
                    need(act, proj_mm, bl.count(4, -4))
                    need(act, v_mm, bl.count(1, -1))
                    copy(xs[:, bl.slot(2), HI, :], xn[:, :]).then_inc(xc_hi, 1)
                    act.wait_ge(c_loaded[bl.slot(2)], bl.rounds(16, 16))
                    copy(cs[:, bl.slot(2), HI, :], c_in[:, bl.slot(2), :]).then_inc(xc_hi, 1)
                if bo.live():
                    high_of_o(bo, 1)
                exps(b2, 6)
                if br.live():
                    act.wait_ge(ntop_done, br.count(1, 1))
                    need(act, rows_done, br.count(3, 0))
                    nc.scalar.activation(ex[:, :], top[:, :], ACT.Exp, bias=ntop[:, 0:1], accum_out=exs[:, 0:1]).then_inc(ex_done, 1)
                exps(b2, 7)

            batch_turns(act, turn)

            def silu(s):
                act.wait_ge(gu_mm, s.count(1, 1))
                need(act, h_done, s.count(1, -1))
                nc.scalar.activation(sil[:, s.slot(2), :], ps[:, s.slot(2), 0:INTER], ACT.Silu, scale=1.0 / WSCALE).then_inc(sil_done, 1)

            def high_of_h(s):
                act.wait_ge(h_done, s.count(1, 1))
                need(act, ht_mm, s.count(1, -1))
                copy(hs[:, s.slot(2), 0:INTER], hf[:, s.slot(2), :]).then_inc(hhi_done, 1)

            def read_ht(s):
                act.wait_ge(ht_mm, s.count(1, 1))
                need(act, d_mm, s.count(1, -1))
                copy(ht[:, s.slot(2), :, :], ps[:, 4 + s.slot(2), :].bitcast(F16)[:, 0:3 * P].rearrange("p (b t) -> p b t", b=3)).then_inc(ht_out, 1)

            def read_y(s):
                act.wait_ge(d_mm, s.count(1, 1))
                need(act, added[s.slot(4)], s.rounds(16, 16))
                copy(y_sb[:, s.slot(4), :], ps[:, 6 + s.slot(2), :], 1.0 / (WSCALE * PSCALE)).then_inc(y_out, 1)

            s0 = Turn(0, 0, 4, STEPS + 8)
            for p in range(2):
                act.wait_ge(x2_stored[p], 16 * (NB // 2))
            act.wait_ge(pv_mm, 8 * NB)
            act.wait_ge(qk_lo, 2 * NB)
            silu(s0)
            high_of_h(s0)
            silu(s0 + 1)
            read_ht(s0)
            high_of_h(s0 + 1)

            def step(s):
                silu(s + 1)
                read_ht(s)
                high_of_h(s + 1)
                read_y(s + -1)

            step_loop(act, step)

        @block.vector
        def _(dve):
            V = nc.vector

            def split(hi, lo, full, scale=1.0):
                return (V.tensor_scalar(hi, full, scale, None, ALU.mult),
                        lambda: V.scalar_tensor_tensor(lo, full, scale, hi, ALU.mult, ALU.subtract))

            V.memset(pad_rows[:, 0:TABLE_ROWS // P * 4], 0).then_inc(pads_set, 1)
            dve.wait_ge(pads_set, 1)
            V.memset(pad_rows[:, 0:TABLE_ROWS // P * 4].rearrange("p (r f) -> p r f", f=4)[:, :, 1], 2 * TOKENS).then_inc(pads_set, 1)
            V.memset(k_st[32:64, :, :, :], MSCALE).then_inc(setup, 1)
            V.memset(v1[:, :, :, :, DH:2 * DH], 1.0).then_inc(setup, 1)
            V.memset(rows[:, :, :, :], 0).then_inc(setup, 1)
            V.memset(zero[:, :], 0.0).then_inc(setup, 1)
            dve.wait_ge(consts_in, 16 * 7)
            a, low = split(pws[:, HI, :, :], pws[:, LO, :, :], pw[:, :, :]); a.then_inc(setup, 1)
            dve.wait_ge(setup, 5); low().then_inc(setup, 1)
            a, low = split(ows[:, HI, :, :], ows[:, LO, :, :], ow[:, :, :]); a.then_inc(setup, 1)
            dve.wait_ge(setup, 7); low().then_inc(setup, 1)
            a, low = split(gws[:, HI, :, :], gws[:, LO, :, :], gw[:, :, :], WSCALE); a.then_inc(setup, 1)
            dve.wait_ge(setup, 9); low().then_inc(setup, 1)
            V.tensor_copy(running[:, :], cf[:, EXPERT_ROW:EXPERT_ROW + E]).then_inc(setup, 1)
            V.tensor_copy(tokf[:, :], cf[:, TOKEN:TOKEN + 1]).then_inc(setup, 1)
            dve.wait_ge(setup, 12)

            def maxima(b, k):
                if not b.live():
                    return
                for h in range(2):
                    pair = 2 * k + h
                    dve.wait_ge(s1_mm, b.count(16, pair + 1))
                    V.tensor_reduce(mx[:, b.slot(2), k, 2 * h:2 * h + 2], ps_m[h], AXX, ALU.max).then_inc(mx_done, 1)
                    yield

            def negate(b, half):
                dve.wait_ge(mx_done, b.count(16, 8 * (half + 1)))
                need(dve, mt_mm, b.count(2, half - 3 + 2))
                V.tensor_scalar(mneg[:, half, 0:16].rearrange("p (h j) -> p h j", h=4), mx[:, b.slot(2), 4 * half:4 * half + 4, :],
                                -1.0 / MSCALE, None, ALU.mult).then_inc(mneg_done, 1)

            def rope(b, n):
                w, swapped = n // 2, n % 2
                dve.wait_ge(proj_mm, b.count(4, n + 1))
                need(dve, rope_sum, b.count(2, w - 1))
                V.scalar_tensor_tensor((rope_b if swapped else rope_a)[:, w, :], ps_x, pb[:, n:n + 1],
                                       cf[:, SIN:SIN + T] if swapped else cf[:, COS:COS + T], ALU.add, ALU.mult).then_inc(rope_done, 1)

            def stats(norm, src, sm, b):
                V.bn_stats(stat[:, norm, 0:6], src).then_inc(sm, 1)
                dve.wait_ge(sm, b.count(3, 1))
                apart(dve)
                V.bn_aggr(mv[:, norm, :], stat[:, norm, 0:6]).then_inc(sm, 1)
                dve.wait_ge(sm, b.count(3, 2))
                V.tensor_scalar(vare[:, norm:norm + 1], mv[:, norm, 1:2], EPS, None, ALU.add).then_inc(sm, 1)

            def reciprocal(b, g):
                dve.wait_ge(den_in, b.count(32, 16 * g + 16))
                need(dve, rcp_out, b.count(32, 16 * g - 16))
                V.reciprocal(rcp[:, g, :], den[:, g, :]).then_inc(rcp_done, 1)

            def scale_o(b, g):
                dve.wait_ge(rcb_in[g], b.count(64, 64))
                dve.wait_ge(o_read, b.count(2, g + 1))
                need(dve, on_lo, b.count(2, g - 1))
                V.tensor_tensor(o_n[:, g, :], o_raw[:, g, :], rcb[:, g, :], ALU.mult).then_inc(on_done, 1)

            def route(b):
                n = [0]

                def link(i):
                    n[0] += 1
                    i.then_inc(rt, 1)
                    dve.wait_ge(rt, b.count(8, n[0]))
                dve.wait_ge(lg_mm, b.count(1, 1))
                V.tensor_scalar(lg[:, :], ps_x[:, 0:E], 1.0 / WSCALE, None, ALU.mult).then_inc(lg_done, 1)
                need(dve, ex_done, b.count(1))
                dve.wait_ge(lg_done, b.count(1, 1))
                apart(dve)
                link(V.max(top[:, :], lg[:, :]))
                V.tensor_scalar(ntop[:, :], top[:, 0:1], -1.0, None, ALU.mult).then_inc(ntop_done, 1)
                link(V.max_index(topi[:, :], top[:, :], lg[:, :]))
                link(V.tensor_copy(topf[:, :], topi[:, :]))
                link(V.tensor_tensor(chosen[:, :, :], cf[:, EXPERT:EXPERT + E].unsqueeze(1).to_broadcast([P, TOPK, E]),
                                     topf[:, :].unsqueeze(2).to_broadcast([P, TOPK, E]), ALU.is_equal))
                need(dve, cnt_mm, b.count(1))
                with nc.allow_low_precision("zeros and ones"):
                    V.tensor_reduce(mask[:, :], chosen[:, :, :].rearrange("p k e -> p e k"), AXX, ALU.add).then_inc(mask_done, 1)
                return link

            def weights(b, link):
                dve.wait_ge(ex_done, b.count(1, 1))
                need(dve, rows_stored[b.slot(2)], b.rounds(16 * TOPK, 0))
                link(V.reciprocal(exr[:, :], exs[:, :]))
                V.tensor_scalar(rows[:, b.slot(2), :, 2].bitcast(F32), ex[:, :], exr[:, 0:1], PSCALE / WSCALE, ALU.mult, ALU.mult).then_inc(rows_done, 1)
                V.tensor_scalar(rows[:, b.slot(2), :, 0:2], zero[:, :].rearrange("p (k f) -> p k f", f=2), tokf[:, 0:1], None, ALU.add).then_inc(rows_done, 1)
                dve.wait_ge(rows_done, b.count(3, 2))
                link(V.tensor_scalar(tokf[:, :], tokf[:, :], float(P), None, ALU.add))

            def places(b, link):
                dve.wait_ge(cnt_mm, b.count(1, 1))
                V.tensor_tensor(place[:, :], ps_x[:, 0:E], running[:, :], ALU.add).then_inc(cnt_done, 1)
                dve.wait_ge(cnt_done, b.count(2, 1))
                V.tensor_tensor(running[:, :], ps_x[:, E:2 * E], running[:, :], ALU.add).then_inc(cnt_done, 1)
                link(V.tensor_tensor(placed[:, :, :], chosen[:, :, :], place[:, :].unsqueeze(1).to_broadcast([P, TOPK, E]), ALU.mult))
                link(V.tensor_reduce(topf[:, :], placed[:, :, :], AXX, ALU.add))
                V.tensor_copy(rowi[:, b.slot(2), :], topf[:, :]).then_inc(rows_done, 1)
                dve.wait_ge(rows_done, b.count(3, 3))

            def turn(it):
                bl, bp, b1, b2, bo, br = it + 3, it + 2, it + 1, it, it + -1, it + -2

                def both(k):
                    for _ in maxima(b1, k):
                        pass
                both(0)
                if bp.live():
                    rope(bp, 0)
                if br.live():
                    stats(1, x2[:, br.slot(2), :], stat2, br)
                if bo.live():
                    scale_o(bo, 0)
                both(1)
                if bp.live():
                    rope(bp, 1)
                if br.live():
                    dve.wait_ge(rstd2, br.count(1, 1))
                    need(dve, x2_lo, br.count(1))
                    V.tensor_scalar(xn2[:, :], x2[:, br.slot(2), :], mv[:, 1, 0:1], rstd[:, 1:2], ALU.subtract, ALU.mult).then_inc(xn2_done, 1)
                both(2)
                if bp.live():
                    rope(bp, 2)
                if bl.live():
                    dve.wait_ge(x_loaded[bl.slot(2)], bl.rounds(16, 16))
                    stats(0, x_in[:, bl.slot(2), :], stat1, bl)
                both(3)
                if bp.live():
                    rope(bp, 3)
                if b1.live():
                    negate(b1, 0)
                if bo.live():
                    reciprocal(bo, 1)
                both(4)
                if bl.live():
                    dve.wait_ge(rstd1, bl.count(1, 1))
                    need(dve, xc_lo, bl.count(1))
                    V.tensor_scalar(xn[:, :], x_in[:, bl.slot(2), :], mv[:, 0, 0:1], rstd[:, 0:1], ALU.subtract, ALU.mult).then_inc(xn_done, 1)
                if b1.live():
                    dve.wait_ge(v_mm, b1.count(1, 1))
                    V.tensor_tensor(v1[:, b1.slot(2), :, :, 0:DH], ps_x.rearrange("p (s h c) -> p s h c", s=NSC, h=HEADS),
                                    vb[:, :].rearrange("p (h c) -> p h c", h=HEADS).unsqueeze(1).to_broadcast([P, NSC, HEADS, DH]), ALU.add).then_inc(v_done, 1)
                if bo.live():
                    scale_o(bo, 1)
                both(5)
                if br.live():
                    link = route(br)
                both(6)
                if b2.live():
                    reciprocal(b2, 0)
                if br.live():
                    weights(br, link)
                    places(br, link)
                both7 = maxima(b1, 7)
                next(both7, None)
                if bo.live():
                    dve.wait_ge(y_mm, bo.count(1, 1))
                    dve.wait_ge(res_loaded[bo.slot(2)], bo.rounds(16, 16))
                    need(dve, x2_stored[bo.slot(2)], bo.rounds(16, 0))
                    V.tensor_tensor(x2[:, bo.slot(2), :], ps_x, x_res[:, bo.slot(2), :], ALU.add).then_inc(x2_done, 1)
                    dve.wait_ge(x2_done, bo.count(1, 1))
                for _ in both7:
                    pass
                if b1.live():
                    negate(b1, 1)

            batch_turns(dve, turn)

            done = [0]

            def link(i):
                done[0] += 1
                i.then_inc(plan_sem, 1)
                dve.wait_ge(plan_sem, done[0])
            link(V.tensor_tensor(plan[:, 0, :], running[:, :], cf[:, EXPERT_ROW:EXPERT_ROW + E], ALU.subtract))
            link(V.tensor_scalar(plani[:, :], plan[:, 0, :], float(P - 1), None, ALU.add))
            link(V.tensor_scalar(plani[:, :], plani[:, :], 7, None, ALU.arith_shift_right))
            link(V.tensor_scalar(plan[:, 1, :], plani[:, :], 1.0, None, ALU.max))
            link(V.tensor_copy(plan[:, 2, :], plan[:, 1, :]))
            at = 2
            for d in (1, 2, 4, 8, 16):
                V.tensor_copy(plan[:, at + 1, 0:d], plan[:, at, 0:d]).then_inc(plan_sem, 1)
                done[0] += 1
                link(V.tensor_tensor(plan[:, at + 1, d:E], plan[:, at, d:E], plan[:, at, 0:E - d], ALU.add))
                at += 1
            for q in range(2):
                step_no = cf[:, STEP_NO + q:STEP_NO + q + 1]
                V.tensor_scalar(plan[:, 8, 0:E - 1], plan[:, at, 0:E - 1], step_no, None, ALU.is_le).then_inc(plan_sem, 1)
                dve.wait_ge(plan_sem, done[0] + 1)
                V.tensor_reduce(col[:, q, 0:1], plan[:, 8, 0:E - 1], AXX, ALU.add).then_inc(plan_sem, 1)
                V.tensor_tensor(plan[:, 9, 0:E - 1], plan[:, 8, 0:E - 1], plan[:, 1, 0:E - 1], ALU.mult).then_inc(plan_sem, 1)
                dve.wait_ge(plan_sem, done[0] + 3)
                done[0] += 3
                link(V.tensor_reduce(col[:, q, 1:2], plan[:, 9, 0:E - 1], AXX, ALU.add))
            c = lambda n: col[:, :, n]
            link(V.tensor_tensor(c(2), cf[:, STEP_NO:STEP_NO + 2], c(1), ALU.subtract))
            nums = [(3, 2, float(P)), (4, 0, float(EROWS))]
            for o, i, m in nums:
                V.tensor_scalar(c(o), c(i), m, None, ALU.mult).then_inc(plan_sem, 1)
                done[0] += 1
            dve.wait_ge(plan_sem, done[0])
            e_int = coli[:, :, 0]
            V.tensor_copy(e_int, c(0)).then_inc(plan_sem, 1)
            done[0] += 1
            dve.wait_ge(plan_sem, done[0])
            ei2 = [(coli[:, :, 1], SLOTS - 1, WCOLS, 1), (coli[:, :, 2], 1, WCOLS, 6)]
            for t, m, _, _ in ei2:
                V.tensor_scalar(t, e_int, m, None, ALU.bitwise_and).then_inc(plan_sem, 1)
                done[0] += 1
            dve.wait_ge(plan_sem, done[0])
            V.tensor_tensor(stepi[:, :, 0], c(3), c(4), ALU.add).then_inc(plan_sem, 1)
            V.tensor_scalar(stepi[:, :, 1], coli[:, :, 1], float(WCOLS), None, ALU.mult).then_inc(plan_sem, 1)
            V.tensor_scalar(stepi[:, :, 2], c(0), 1.0, None, ALU.add).then_inc(plan_sem, 1)
            V.tensor_scalar(stepi[:, :, 3], c(2), 0.0, None, ALU.is_equal).then_inc(plan_sem, 1)
            V.tensor_copy(stepi[:, :, 4], c(1)).then_inc(plan_sem, 1)
            V.tensor_scalar(stepi[:, :, 5], coli[:, :, 2], -float(WCOLS), float(WCOLS), ALU.mult, ALU.add).then_inc(plan_sem, 1)
            V.tensor_scalar(stepi[:, :, 6], coli[:, :, 2], float(WCOLS), None, ALU.mult).then_inc(plan_sem, 1)
            V.tensor_scalar(stepi[:, :, 7], c(0), 2.0, float(E - 1), ALU.add, ALU.min).then_inc(plan_sem, 1)
            done[0] += 8
            assert done[0] == PLAN_STEPS

            dve.wait_ge(tab_in, 16)
            for p in range(2):
                dve.wait_ge(x2_stored[p], 16 * (NB // 2))
            dve.wait_ge(pv_mm, 8 * NB)
            dve.wait_ge(qk_lo, 2 * NB)

            def split_weights(src, dst):
                hi = V.tensor_scalar(w_hi[:, dst], stage[:, src], WSCALE, None, ALU.mult)
                hi.then_inc(w_split, 1)
                return lambda: V.scalar_tensor_tensor(w_lo[:, dst], stage[:, src], WSCALE, w_hi[:, dst], ALU.mult, ALU.subtract).then_inc(w_split, 1)

            for n in range(2):
                dve.wait_ge(w_in, 16 * (n + 1))
                low = split_weights(slice(n * WCOLS, (n + 1) * WCOLS), slice(n * WCOLS, (n + 1) * WCOLS))
                dve.wait_ge(w_split, 2 * n + 1)
                low()

            def next_weights(s):
                first = field(dve, s + 1, 3, 0, 1)
                with dve.If(first > 0):
                    e1 = field(dve, s + 1, 2, 1, E)
                    src = field(dve, s + 1, 5, 0, WCOLS)
                    slot = dve.snap((e1 % SLOTS) * WCOLS, max_val=(SLOTS - 1) * WCOLS)
                    dve.wait_ge(w_in, e1 * 16 + 16)
                    low = split_weights(bass.ds(src, WCOLS), bass.ds(slot, WCOLS))
                    dve.wait_ge(w_split, e1 * 2 + 1)
                    low()
                with dve.Else():
                    dve.nop()
                dve.nop()

            def read_xt(s):
                dve.wait_ge(xgt_mm, s.count(1, 1))
                need(dve, gu_mm, s.count(1, -1))
                V.tensor_copy(xt[:, s.slot(2), :], ps[:, 2 + s.slot(2), :].bitcast(F16)).then_inc(xt_out, 1)

            def hidden(s):
                dve.wait_ge(sil_done, s.count(1, 1))
                dve.wait_ge(sidx_in[s.slot(4)], s.rounds(16, 16))
                need(dve, hhi_done, s.count(1, -1))
                need(dve, hlo_done, s.count(1, -1))
                V.scalar_tensor_tensor(hf[:, s.slot(2), :], sil[:, s.slot(2), :], s_idx[:, s.slot(4), 2:3].bitcast(F32),
                                       ps[:, s.slot(2), INTER:2 * INTER], ALU.mult, ALU.mult).then_inc(h_done, 1)

            def low_of_h(s):
                dve.wait_ge(hhi_done, s.count(1, 1))
                V.tensor_tensor(hs[:, s.slot(2), INTER:2 * INTER], hf[:, s.slot(2), :], hs[:, s.slot(2), 0:INTER], ALU.subtract).then_inc(hlo_done, 1)

            s0 = Turn(0, 0, 4, STEPS + 8)
            read_xt(s0)
            read_xt(s0 + 1)
            hidden(s0)
            low_of_h(s0)
            next_weights(s0)
            read_xt(s0 + 2)
            hidden(s0 + 1)
            low_of_h(s0 + 1)

            def step(s):
                read_xt(s + 2)
                hidden(s + 1)
                low_of_h(s + 1)
                next_weights(s)

            step_loop(dve, step)

        @block.tensor
        def _(pe):
            mm = nc.tensor.matmul
            PARTS = ((HI, HI), (HI, LO), (LO, HI))
            pe.wait_ge(setup, 12)

            def project(b, n):
                if not b.live():
                    return
                src = xs if n < 2 else cs
                if n == 0:
                    pe.wait_ge(xc_lo, b.count(1, 1))
                for m, (pw_, px) in enumerate(PARTS):
                    last = mm(ps_x, pws[:, pw_, n, :], src[:, b.slot(2), px, :], start=(m == 0), stop=(m == 2))
                last.then_inc(proj_mm, 1)

            def values(b):
                need(pe, pv_mm, b.count(8, -8))
                for s in range(NSC):
                    for m, (pc, pw_) in enumerate(PARTS):
                        last = mm(ps_x[:, s * P:(s + 1) * P], cs[:, b.slot(2), pc, s * P:(s + 1) * P], pws[:, pw_, 4, :], start=(m == 0), stop=(m == 2))
                last.then_inc(v_mm, 1)

            def output(b):
                pe.wait_ge(on_lo, b.count(2, 2))
                m = 0
                for g in range(2):
                    for pw_, po in PARTS:
                        last = mm(ps_x, ows[:, pw_, g, :], o_s[:, g, po, :], start=(m == 0), stop=(m == 5))
                        m += 1
                last.then_inc(y_mm, 1)

            def max_rows(b, half):
                pe.wait_ge(mneg_done, b.count(2, half + 1))
                nc.tensor.transpose(ps_xh[0:16, 0:P], mneg[:, half, 0:16], ident).then_inc(mt_mm, 1)

            def tokens_transposed(b):
                pe.wait_ge(x2_lo, b.count(1, 1))
                for n in range(8):
                    last = nc.tensor.transpose(ps_xh[:, n * P:(n + 1) * P], x2s[:, b.slot(2), n // KT, n % KT * P:(n % KT + 1) * P], ident)
                last.then_inc(xt_mm, 1)

            def logits(b):
                pe.wait_ge(xt_read, b.count(1, 1))
                m = 0
                for px, pg in PARTS:
                    for k in range(KT):
                        last = mm(ps_x[:, 0:E], x2t[:, px * KT + k, :], gws[:, pg, k, :], start=(m == 0), stop=(m == 3 * KT - 1))
                        m += 1
                last.then_inc(lg_mm, 1)

            def counts(b):
                pe.wait_ge(mask_done, b.count(1, 1))
                mm(ps_x[:, 0:E], before, mask[:, :], start=True, stop=True)
                mm(ps_x[:, E:2 * E], ones, mask[:, :], start=True, stop=True).then_inc(cnt_mm, 1)

            def turn(it):
                bp, b1, b2, bo, br = it + 2, it + 1, it, it + -1, it + -2
                small = {(0, 0): ("q", bp, lambda: project(bp, 0)), (0, 3): ("mt1", b2, lambda: max_rows(b2, 1)),
                         (1, 0): ("qr", bp, lambda: project(bp, 1)), (2, 0): ("k", bp, lambda: project(bp, 2)),
                         (3, 0): ("kr", bp, lambda: project(bp, 3)), (4, 0): ("xt", br, lambda: tokens_transposed(br)),
                         (4, 3): ("mt0", b1, lambda: max_rows(b1, 0)), (5, 0): ("v", b1, lambda: values(b1)),
                         (5, 3): ("lg", br, lambda: logits(br)), (6, 3): ("cnt", br, lambda: counts(br)),
                         (7, 1): ("y", bo, lambda: output(bo))}
                for k in range(8):
                    for i in range(4):
                        if b2.live():
                            h, sc = 4 * (k // 4) + i, k % NSC
                            if i == 0 and sc == 0:
                                pe.wait_ge(mrow_in[b2.slot(2)][k // 4], b2.rounds(16, 16))
                            need(pe, exp_done, b2.count(32, 4 * k + i - 1))
                            mm(ps_s[i % 2], k_st[0:SHARE + 1, b2.slot(2), h, sc * P:(sc + 1) * P], q_st[0:SHARE + 1, b2.slot(2), h, :],
                               start=True, stop=True).then_inc(s2_mm, 1)
                        bv, kv = (bo, 7) if k == 0 else (b2, k - 1)
                        if bv.live():
                            if i == 0:
                                pe.wait_ge(exp_done, bv.count(32, 4 * kv + 4))
                                if kv % NSC == 0:
                                    need(pe, o_read, bv.count(2, kv // NSC))
                                if kv == 0:
                                    pe.wait_ge(v_done, bv.count(1, 1))
                            last = mm(ps_o[2 * DH * i:2 * DH * (i + 1), :], v1[:, bv.slot(2), kv % NSC, 4 * (kv // NSC) + i, :],
                                      pr[:, (4 * kv + i) % 8, :], start=(kv % NSC == 0), stop=(kv % NSC == NSC - 1))
                            if i == 3:
                                last.then_inc(pv_mm, 1)
                        if b1.live():
                            if i == 0 and k % 4 == 0:
                                pe.wait_ge(stack_in[b1.slot(2)][k // 4], b1.rounds(96, 96))
                            if i % 2 == 0:
                                need(pe, mx_done, b1.count(16, 2 * k + i // 2 - 1))
                            last = mm(ps_m[i // 2][:, i % 2, :], q_st[0:SHARE, b1.slot(2), k, i * P:(i + 1) * P], k_st[0:SHARE, b1.slot(2), k, :],
                                      start=True, stop=True)
                            if i % 2 == 1:
                                last.then_inc(s1_mm, 1)
                        if (k, i) in small:
                            name, b, work = small[k, i]
                            if b.live():
                                bank_is_free(pe, it, name)
                                work()

            batch_turns(pe, turn)

            pe.wait_ge(tab_in, 16)
            pe.wait_ge(xt_read, NB)
            pe.wait_ge(x2_done, NB)
            pe.wait_ge(cnt_done, 2 * NB)
            pe.wait_ge(mx_done, 16 * NB)

            def gate_up(s):
                slot = field(pe, s, 1, 0, (SLOTS - 1) * WCOLS)
                pe.wait_ge(w_split, field(pe, s, 2, 1, E) * 2)
                pe.wait_ge(xt_out, s.count(1, 1))
                need(pe, h_done, s.count(1, -1))
                m = 0
                for k in range(KT):
                    cols = bass.ds(slot + k * 2 * INTER, 2 * INTER)
                    for px, w in ((HI, w_hi), (HI, w_lo), (LO, w_hi)):
                        at = (px * KT + k) * P
                        last = mm(ps[:, s.slot(2), 0:2 * INTER], xt[:, s.slot(2), at:at + P], w[:, cols], start=(m == 0), stop=(m == 3 * KT - 1))
                        m += 1
                last.then_inc(gu_mm, 1)

            def transpose_x(s):
                pe.wait_ge(gathered[s.slot(4)], s.rounds(16, 16))
                need(pe, xt_out, s.count(1, -1))
                for n in range(8):
                    last = nc.tensor.transpose(ps[:, 2 + s.slot(2), :].bitcast(F16)[:, n * P:(n + 1) * P], xg[:, s.slot(4), n * P:(n + 1) * P], ident)
                last.then_inc(xgt_mm, 1)

            def transpose_h(s):
                pe.wait_ge(hlo_done, s.count(1, 1))
                need(pe, ht_out, s.count(1, -1))
                o = ps[:, 4 + s.slot(2), :].bitcast(F16)
                both = hs[:, s.slot(2), :].rearrange("p (a b) -> p a b", a=2)
                nc.tensor.transpose(o[:, 0:P], both[:, HI, 0:P], ident)
                nc.tensor.transpose(o[:, P:2 * P], both[:, LO, 0:P], ident)
                nc.tensor.transpose(o[0:INTER - P, 2 * P:3 * P], both[:, HI, P:INTER], ident)
                nc.tensor.transpose(o[INTER - P:P, 2 * P:3 * P], both[:, LO, P:INTER], ident).then_inc(ht_mm, 1)

            def down(s):
                slot = field(pe, s, 1, 0, (SLOTS - 1) * WCOLS)
                pe.wait_ge(ht_out, s.count(1, 1))
                need(pe, y_out, s.count(1, -1))
                y = ps[:, 6 + s.slot(2), :]
                h = ht[:, s.slot(2), :, :]
                d0, d1 = slot + DOWN, slot + (DOWN + T)
                mm(y, h[:, 0, :], w_hi[:, bass.ds(d0, T)], start=True, stop=False)
                mm(y, h[:, 0, :], w_lo[:, bass.ds(d0, T)], start=False, stop=False)
                mm(y, h[:, 1, :], w_hi[:, bass.ds(d0, T)], start=False, stop=False)
                mm(y, h[:, 2, :], w_hi[:, bass.ds(d1, T)], start=False, stop=False)
                mm(y, h[0:64, 2, :], w_lo[0:64, bass.ds(d1, T)], start=False, stop=True).then_inc(d_mm, 1)

            s0 = Turn(0, 0, 4, STEPS + 8)
            transpose_x(s0)
            transpose_x(s0 + 1)
            gate_up(s0)
            gate_up(s0 + 1)
            transpose_x(s0 + 2)
            transpose_h(s0)

            def step(s):
                gate_up(s + 1)
                transpose_x(s + 2)
                transpose_h(s)
                down(s + -1)

            step_loop(pe, step)


_INS = ["x", "ctx", "proj_w", "proj_b", "value_b", "out_w", "gate_w", "expert_w", "const_f", "const_h"]


def _layout(inp):
    f = lambda n: np.asarray(inp[n])
    o = np.arange(P)
    swap = o // DH * DH + (o % DH + DH // 2) % DH
    wq, wk, wv, wo = (f(f"L0_xattn_W{n}") for n in "qkvo")
    bq, bk, bv, bo = (f(f"L0_xattn_b{n}") for n in "qkvo")
    proj_w = np.stack([wq.T, wq[swap].T, wk.T, wk[swap].T, wv.T], axis=1)
    proj_b = np.stack([bq, bq[swap], bk, bk[swap]], axis=1)
    out_w = np.zeros((P, 2, P), wo.dtype)
    for g in range(2):
        for j in range(4):
            h = 4 * g + j
            out_w[2 * DH * j:2 * DH * j + DH, g, :] = wo[:, h * DH:(h + 1) * DH].T
    out_w[DH, 0, :] = bo
    gate = f("L0_ffn_gate_w").T.reshape(KT, P, E).transpose(1, 0, 2)
    gp, up, dn = f("L0_ffn_w_gate_proj"), f("L0_ffn_w_up_proj"), f("L0_ffn_w_down_proj")
    gu = np.concatenate([gp, up], axis=1).transpose(0, 2, 1).reshape(E, KT, P, 2 * INTER).transpose(0, 2, 1, 3).reshape(E, P, -1)
    dt = dn.transpose(0, 2, 1)
    rest = dt[:, P:INTER]
    expert_w = np.concatenate([gu, dt[:, 0:P], np.concatenate([rest, rest], axis=1)], axis=2)
    const_f, const_h = _constants(f("x").shape[0])
    arrays = dict(x=f("x"), ctx=f("ctx_2048"), proj_w=proj_w, proj_b=proj_b, value_b=np.repeat(bv[None], P, axis=0),
                  out_w=out_w, gate_w=gate, expert_w=expert_w, const_f=const_f, const_h=const_h)
    return {k: np.ascontiguousarray(v) for k, v in arrays.items()}


def _constants(nb):
    inv = (1.0 / 10000.0 ** (np.arange(0, DH, 2, dtype=np.float32) / DH)).astype(np.float32)
    angle = (np.arange(T, dtype=np.float32)[None, :] * np.tile(inv, 2 * HEADS)[:, None]).astype(np.float32)
    sign = np.where(np.arange(P) % DH < DH // 2, -1.0, 1.0)[:, None]
    c = np.zeros((P, NCONST), np.float32)
    c[:, COS:COS + T] = np.cos(angle.astype(np.float64))
    c[:, SIN:SIN + T] = np.sin(angle.astype(np.float64)) * sign
    c[:, EXPERT:EXPERT + E] = np.arange(E)
    c[:, EXPERT_ROW:EXPERT_ROW + E] = np.arange(E) * (nb * P)
    c[:, STEP_NO:STEP_NO + 2] = np.arange(P)[:, None] + np.array([0, P])
    c[:, TOKEN] = np.arange(P)
    c[:, HALF] = -0.5
    h = np.stack([np.eye(P), np.triu(np.ones((P, P)), 1), np.ones((P, P))], axis=1).astype(np.float16)
    return c, h


def kernel(**inputs):
    import concourse.bacc as bacc
    from concourse.bass_utils import run_bass_kernel_spmd

    laid = _layout(inputs)
    nc = bacc.Bacc("TRN2", target_bir_lowering=False, num_devices=1)
    arrays, args = {}, []
    for name in _INS:
        arrays[f"in_{name}"] = laid[name]
        args.append(nc.dram_tensor(f"in_{name}", laid[name].shape, mybir.dt.from_np(laid[name].dtype), kind="ExternalInput").ap())
    out = nc.dram_tensor("out", laid["x"].shape, F32, kind="ExternalOutput").ap()
    xattn_moe(nc, *args, out)
    r = run_bass_kernel_spmd(nc, [arrays], core_ids=[0])
    return r.results[0]["out"]
```
